# Optimizing a Trainium2 kernel written in Bass

```python
import numpy as np
import jax
import jax.numpy as jnp

def _softmax(x, axis=-1):
    return jax.nn.softmax(x, axis=axis)

def _gelu(x):
    return jax.nn.gelu(x, approximate=True)

def _silu(x):
    return jax.nn.silu(x)

def _sigmoid(x):
    return jax.nn.sigmoid(x)

def _layernorm(x, axis=-1, eps=1e-05):
    m = jnp.mean(x, axis=axis, keepdims=True)
    v = jnp.var(x, axis=axis, keepdims=True)
    return (x - m) / jnp.sqrt(v + eps)

def _scatter_add(tgt, idx, src, axis=0):
    return tgt.at[idx].add(src)

def _segment_sum(src, seg, n):
    return jax.ops.segment_sum(src, seg, n)
kernel_name = 'mk_dlrm_tower_d1_rec_r8_51883a'

def setup_inputs(seed: int=0):
    np.random.seed(seed)
    _w = jnp.asarray

    def _rec_inputs():
        import jax
        import jax.numpy as jnp
        _tk = jax.random.key(seed)
        ids = jnp.stack([jax.random.randint(jax.random.fold_in(_tk, 200 + f), (2048,), 0, v, jnp.int32) for f, v in enumerate([1000, 12500, 125000, 1000, 1250, 12500, 1250, 1000, 12500, 1000, 1250, 1250, 1000, 1000, 1000, 1000, 12500, 1000, 1000, 12500, 1000, 12500, 12500, 1000, 1000, 1250])], axis=1)
        tbl_0 = 0.05 * jax.random.normal(jax.random.fold_in(_tk, 500 + 0), (1000, 128), jnp.float32)
        tbl_1 = 0.05 * jax.random.normal(jax.random.fold_in(_tk, 500 + 1), (12500, 128), jnp.float32)
        tbl_2 = 0.05 * jax.random.normal(jax.random.fold_in(_tk, 500 + 2), (125000, 128), jnp.float32)
        tbl_3 = 0.05 * jax.random.normal(jax.random.fold_in(_tk, 500 + 3), (1000, 128), jnp.float32)
        tbl_4 = 0.05 * jax.random.normal(jax.random.fold_in(_tk, 500 + 4), (1250, 128), jnp.float32)
        tbl_5 = 0.05 * jax.random.normal(jax.random.fold_in(_tk, 500 + 5), (12500, 128), jnp.float32)
        tbl_6 = 0.05 * jax.random.normal(jax.random.fold_in(_tk, 500 + 6), (1250, 128), jnp.float32)
        tbl_7 = 0.05 * jax.random.normal(jax.random.fold_in(_tk, 500 + 7), (1000, 128), jnp.float32)
        tbl_8 = 0.05 * jax.random.normal(jax.random.fold_in(_tk, 500 + 8), (12500, 128), jnp.float32)
        tbl_9 = 0.05 * jax.random.normal(jax.random.fold_in(_tk, 500 + 9), (1000, 128), jnp.float32)
        tbl_10 = 0.05 * jax.random.normal(jax.random.fold_in(_tk, 500 + 10), (1250, 128), jnp.float32)
        tbl_11 = 0.05 * jax.random.normal(jax.random.fold_in(_tk, 500 + 11), (1250, 128), jnp.float32)
        tbl_12 = 0.05 * jax.random.normal(jax.random.fold_in(_tk, 500 + 12), (1000, 128), jnp.float32)
        tbl_13 = 0.05 * jax.random.normal(jax.random.fold_in(_tk, 500 + 13), (1000, 128), jnp.float32)
        tbl_14 = 0.05 * jax.random.normal(jax.random.fold_in(_tk, 500 + 14), (1000, 128), jnp.float32)
        tbl_15 = 0.05 * jax.random.normal(jax.random.fold_in(_tk, 500 + 15), (1000, 128), jnp.float32)
        tbl_16 = 0.05 * jax.random.normal(jax.random.fold_in(_tk, 500 + 16), (12500, 128), jnp.float32)
        tbl_17 = 0.05 * jax.random.normal(jax.random.fold_in(_tk, 500 + 17), (1000, 128), jnp.float32)
        tbl_18 = 0.05 * jax.random.normal(jax.random.fold_in(_tk, 500 + 18), (1000, 128), jnp.float32)
        tbl_19 = 0.05 * jax.random.normal(jax.random.fold_in(_tk, 500 + 19), (12500, 128), jnp.float32)
        tbl_20 = 0.05 * jax.random.normal(jax.random.fold_in(_tk, 500 + 20), (1000, 128), jnp.float32)
        tbl_21 = 0.05 * jax.random.normal(jax.random.fold_in(_tk, 500 + 21), (12500, 128), jnp.float32)
        tbl_22 = 0.05 * jax.random.normal(jax.random.fold_in(_tk, 500 + 22), (12500, 128), jnp.float32)
        tbl_23 = 0.05 * jax.random.normal(jax.random.fold_in(_tk, 500 + 23), (1000, 128), jnp.float32)
        tbl_24 = 0.05 * jax.random.normal(jax.random.fold_in(_tk, 500 + 24), (1000, 128), jnp.float32)
        tbl_25 = 0.05 * jax.random.normal(jax.random.fold_in(_tk, 500 + 25), (1250, 128), jnp.float32)
        _rk = jax.random.fold_in(_tk, 7)
        r_dense_features = -0.000520686 + 1.00062 * jax.random.normal(jax.random.fold_in(_rk, 101), (2048, 128), jnp.float32)
        W_top1 = 0.0405887 * jax.random.normal(jax.random.fold_in(_tk, 801), (607, 512), jnp.float32)
        W_top2 = 0.0441942 * jax.random.normal(jax.random.fold_in(_tk, 802), (512, 256), jnp.float32)
        W_top3 = 0.0625 * jax.random.normal(jax.random.fold_in(_tk, 803), (256, 1), jnp.float32)
        b_top1 = jnp.zeros((512,), jnp.float32)
        b_top2 = jnp.zeros((256,), jnp.float32)
        return (r_dense_features, ids, tbl_0, tbl_1, tbl_2, tbl_3, tbl_4, tbl_5, tbl_6, tbl_7, tbl_8, tbl_9, tbl_10, tbl_11, tbl_12, tbl_13, tbl_14, tbl_15, tbl_16, tbl_17, tbl_18, tbl_19, tbl_20, tbl_21, tbl_22, tbl_23, tbl_24, tbl_25, W_top1, b_top1, W_top2, b_top2, W_top3)
    r_dense_features, ids, tbl_0, tbl_1, tbl_2, tbl_3, tbl_4, tbl_5, tbl_6, tbl_7, tbl_8, tbl_9, tbl_10, tbl_11, tbl_12, tbl_13, tbl_14, tbl_15, tbl_16, tbl_17, tbl_18, tbl_19, tbl_20, tbl_21, tbl_22, tbl_23, tbl_24, tbl_25, W_top1, b_top1, W_top2, b_top2, W_top3 = _rec_inputs()

    def _L0_rec_setup():
        import jax, jax.numpy as jnp
        import numpy as np
        B, F, D = (2048, 26, 128)
        key = jax.random.key(seed)
        k1, k2 = jax.random.split(key)
        dense_features = jax.random.normal(k1, (B, D), dtype=jnp.float32)
        sparse_values = jax.random.normal(k2, (B, F, D), dtype=jnp.float32)
        return {'dense_features': dense_features, 'sparse_values': sparse_values}
    _L0_rec_all = _L0_rec_setup()
    _L0_rec_in = {k: v for k, v in _L0_rec_all.items() if k in ()}
    del _L0_rec_all
    return {'r_dense_features': r_dense_features, 'ids': ids, 'tbl_0': tbl_0, 'tbl_1': tbl_1, 'tbl_2': tbl_2, 'tbl_3': tbl_3, 'tbl_4': tbl_4, 'tbl_5': tbl_5, 'tbl_6': tbl_6, 'tbl_7': tbl_7, 'tbl_8': tbl_8, 'tbl_9': tbl_9, 'tbl_10': tbl_10, 'tbl_11': tbl_11, 'tbl_12': tbl_12, 'tbl_13': tbl_13, 'tbl_14': tbl_14, 'tbl_15': tbl_15, 'tbl_16': tbl_16, 'tbl_17': tbl_17, 'tbl_18': tbl_18, 'tbl_19': tbl_19, 'tbl_20': tbl_20, 'tbl_21': tbl_21, 'tbl_22': tbl_22, 'tbl_23': tbl_23, 'tbl_24': tbl_24, 'tbl_25': tbl_25, 'W_top1': W_top1, 'b_top1': b_top1, 'W_top2': W_top2, 'b_top2': b_top2, 'W_top3': W_top3}

def reference(r_dense_features, ids, tbl_0, tbl_1, tbl_2, tbl_3, tbl_4, tbl_5, tbl_6, tbl_7, tbl_8, tbl_9, tbl_10, tbl_11, tbl_12, tbl_13, tbl_14, tbl_15, tbl_16, tbl_17, tbl_18, tbl_19, tbl_20, tbl_21, tbl_22, tbl_23, tbl_24, tbl_25, W_top1, b_top1, W_top2, b_top2, W_top3):
    import jax
    import jax.numpy as jnp

    def _L0_rec_ref(dense_features, sparse_values):
        import jax, jax.numpy as jnp
        import numpy as np
        B, F, D = (2048, 26, 128)
        sd = jnp.einsum('bfd,bd->bf', sparse_values, dense_features)
        ss = jnp.einsum('bfd,bgd->bfg', sparse_values, sparse_values)
        iu, ju = jnp.triu_indices(F, k=1)
        pairs = ss[:, iu, ju]
        return jnp.concatenate([dense_features, sd, pairs], axis=1)
    e = jnp.stack([tbl_0[ids[:, 0]], tbl_1[ids[:, 1]], tbl_2[ids[:, 2]], tbl_3[ids[:, 3]], tbl_4[ids[:, 4]], tbl_5[ids[:, 5]], tbl_6[ids[:, 6]], tbl_7[ids[:, 7]], tbl_8[ids[:, 8]], tbl_9[ids[:, 9]], tbl_10[ids[:, 10]], tbl_11[ids[:, 11]], tbl_12[ids[:, 12]], tbl_13[ids[:, 13]], tbl_14[ids[:, 14]], tbl_15[ids[:, 15]], tbl_16[ids[:, 16]], tbl_17[ids[:, 17]], tbl_18[ids[:, 18]], tbl_19[ids[:, 19]], tbl_20[ids[:, 20]], tbl_21[ids[:, 21]], tbl_22[ids[:, 22]], tbl_23[ids[:, 23]], tbl_24[ids[:, 24]], tbl_25[ids[:, 25]]], axis=1)
    z = _L0_rec_ref(r_dense_features, e)
    z = z.reshape(z.shape[0], -1)
    h = jnp.concatenate([z, r_dense_features], axis=1)
    h = jnp.maximum(h @ W_top1 + b_top1, 0.0)
    h = jnp.maximum(h @ W_top2 + b_top2, 0.0)
    y = h @ W_top3
    return y

_drawn_inputs = setup_inputs


def setup_inputs(seed=0):
    import zlib

    import numpy as np

    out = dict(_drawn_inputs(seed))
    spreads = {'b_top1': (0.0, 0.1), 'b_top2': (0.0, 0.1)}
    factors = {}
    for name, (base, spread) in spreads.items():
        noise = np.random.default_rng([zlib.crc32(name.encode()), seed]).standard_normal(out[name].shape)
        drawn = base * np.exp(spread * noise) if base else spread * noise
        out[name] = jnp.asarray(drawn.astype(out[name].dtype))
    for name, factor in factors.items():
        out[name] = (out[name] * factor).astype(out[name].dtype)
    return out
```

```python
import concourse.bass as bass
from concourse import mybir
from contextlib import ExitStack


def dlrm_tower_kernel(nc, dense, ids, tables, W_top1, b_top1, W_top2, b_top2, W_top3, y):
    fp32 = mybir.dt.float32
    int32 = mybir.dt.int32
    ALU = mybir.AluOpType
    ACT = mybir.ActivationFunctionType

    P = 128
    B, D = dense.shape
    F = len(tables)
    ITEMS = F + 1
    N1, N2 = W_top1.shape[1], W_top2.shape[1]
    BS = 512
    S = B // BS
    T = BS // P
    GS = 4
    SLOT = P // GS
    GT = P // GS
    FG = 8
    GFILLS = GT // FG
    QUAD = 4
    QUADS = -(-ITEMS // QUAD)
    quad = [list(range(QUAD * k, min(QUAD * k + QUAD, ITEMS))) for k in range(QUADS)]
    looked_up = [[f for f in q if f < F] for q in quad]
    PAIRS = F * (F - 1) // 2
    Z = F + PAIRS
    ZC = 3
    ZK = Z // ZC
    assert ZC * ZK == Z and ZK <= P
    pair_row = [F + f * (F - 1) - f * (f - 1) // 2 for f in range(F)]
    gcols = [F] + list(range(F - 1))
    UQ = 4
    UFILLS = -(-len(gcols) // UQ)
    M1, M2 = N1 // P, N2 // P

    U0, V0 = 0, UFILLS
    L1_0 = V0 + ZC
    L2_0 = L1_0 + M1
    L3_0 = L2_0 + M2
    XFILLS = L3_0 + 1

    ctx = ExitStack()
    with ctx:
        def sb(name, shape, dt=fp32):
            return ctx.enter_context(nc.sbuf_tensor(name, shape, dt))

        def pb(name, shape):
            return ctx.enter_context(nc.psum_tensor(name, shape, fp32))

        def sem(name):
            return ctx.enter_context(nc.semaphore(name))

        ids_sb = sb("ids_sb", [P, T, F], int32)
        rows = [sb(f"rows{j}", [P, F, D]) for j in range(2)]
        dense_sb = sb("dense_sb", [P, T, D])
        eT = [sb(f"eT{j}", [P, P, SLOT]) for j in range(2)]
        dT = sb("dT", [P, GS, T, GT])
        gramZ = sb("gramZ", [P, ITEMS, P])
        feats = sb("feats", [P, GS, Z])
        featsT = sb("featsT", [ZK, ZC, BS])
        h1T = sb("h1T", [P, M1, BS])
        h2T = sb("h2T", [P, M2, BS])
        y_sb = sb("y_sb", [P, GS])
        w1 = sb("w1", [ZK, ZC, N1])
        w1d = sb("w1d", [P, 2, N1])
        w1s = sb("w1s", [P, N1])
        w2 = sb("w2", [P, M1, N2])
        w3 = sb("w3", [P, M2])
        b1 = sb("b1", [P, M1])
        b2 = sb("b2", [P, M2])
        ident = sb("ident", [P, P])

        tp = [pb(f"tp{j}", [P, QUAD, P]) for j in range(2)]
        gm = [pb(f"gm{j}", [P, FG, P]) for j in range(2)]
        mx = [pb(f"mx{j}", [P, BS]) for j in range(2)]

        ids_in = [sem(f"ids_in{t}") for t in range(T)]
        dense_in = sem("dense_in")
        w1_in = sem("w1_in")
        w1d_in = sem("w1d_in")
        tail_in = sem("tail_in")
        y_out = sem("y_out")
        rows_in = [[sem(f"rows_in{j}_{k}") for k in range(QUADS)] for j in range(2)]
        pool_steps = sem("pool_steps")
        ident_zero = sem("ident_zero")
        ident_ok = sem("ident_ok")
        slots_zero = sem("slots_zero")
        w1s_ok = sem("w1s_ok")
        turned = sem("turned")
        turned_copied = sem("turned_copied")
        gram_done = sem("gram_done")
        gram_copied = sem("gram_copied")
        regrouped = sem("regrouped")
        feats_copied = sem("feats_copied")
        feats_turned = sem("feats_turned")
        featsT_copied = sem("featsT_copied")
        h1_done = sem("h1_done")
        h1_copied = sem("h1_copied")
        h2_done = sem("h2_done")
        h2_copied = sem("h2_copied")
        y_done = sem("y_done")
        y_copied = sem("y_copied")

        block = ctx.enter_context(nc.Block())

        def blocks(eng, body):
            body(0, True)
            with eng.Fori(1, S) as s:
                body(s, False)

        @block.sync
        def _(sp):
            for t in range(T):
                sp.dma_start(ids_sb[:, t, :], ids[P * t:P * t + P, :]).then_inc(ids_in[t], 16)
            dense_t = dense.rearrange("(n p) d -> p n d", p=P)
            sp.dma_start(dense_sb[:, :, :], dense_t[:, 0:T, :]).then_inc(dense_in, 16)
            sp.dma_start(w1[:, :, :], W_top1[D:D + Z, :].rearrange("(k p) n -> p k n", p=ZK)).then_inc(w1_in, 16)
            sp.dma_start(w1d[:, 0, :], W_top1[0:D, :]).then_inc(w1d_in, 16)
            sp.dma_start(w1d[:, 1, :], W_top1[D + Z:D + Z + D, :]).then_inc(w1d_in, 16)
            sp.dma_start(w2[:, :, :], W_top2.rearrange("(k p) n -> p k n", p=P)).then_inc(tail_in, 16)
            with nc.allow_non_contiguous_dma(reason="a few hundred words, once"):
                sp.dma_start(w3[:, :], W_top3.rearrange("(k p) n -> p (k n)", p=P)).then_inc(tail_in, 16)
                sp.dma_start(b1[:, :], b_top1.rearrange("(k p) -> p k", p=P)).then_inc(tail_in, 16)
                sp.dma_start(b2[:, :], b_top2.rearrange("(k p) -> p k", p=P)).then_inc(tail_in, 16)
            with sp.Fori(1, S) as s:
                for t in range(T):
                    sp.wait_ge(turned, T * QUADS * (s - 1) + QUADS * (t + 1))
                    sp.dma_start(ids_sb[:, t, :], ids[bass.ds(BS * s + P * t, P), :]).then_inc(ids_in[t], 16)
                sp.wait_ge(turned, T * QUADS * s)
                sp.dma_start(dense_sb[:, :, :], dense_t[:, bass.ds(T * s, T), :]).then_inc(dense_in, 16)
            sp.wait_ge(y_out, 16 * S)

        @block.gpsimd
        def _(pool):
            pool.memset(ident[:, :], 0.0).then_inc(ident_zero, 1)
            pool.wait_ge(ident_zero, 1)
            pool.affine_select(out=ident[:, :], in_=ident[:, :], compare_op=ALU.not_equal, fill=1.0,
                               base=0, pattern=[[-1, P]], channel_multiplier=1).then_inc(ident_ok, 1)
            def lookups(s, first):
                for t in range(T):
                    pool.wait_ge(ids_in[t], 16 * s + 16)
                    pool.sem_inc(pool_steps, 1)
                    for k in range(QUADS):
                        if not (first and t < 2):
                            pool.wait_ge(turned, T * QUADS * s + QUADS * (t - 2) + k + 1)
                            pool.sem_inc(pool_steps, 1)
                        for f in looked_up[k]:
                            pool.indirect_dma_start(
                                rows[t % 2][:, f, :], None, tables[f],
                                bass.IndirectOffsetOnAxis(ids_sb[:, t, f:f + 1], 0)
                            ).then_inc(rows_in[t % 2][k], 16)

            blocks(pool, lookups)

        @block.tensor
        def _(pe):
            def shared_bank_free(s, first, n):
                m = n - 2
                if m < 0:
                    if first:
                        return
                    m, s = (XFILLS - 1 if n == XFILLS % 2 else XFILLS - 2), s - 1
                if m < V0:
                    pe.wait_ge(feats_copied, UFILLS * s + m - U0 + 1)
                elif m < L1_0:
                    pe.wait_ge(featsT_copied, ZC * s + m - V0 + 1)
                elif m < L2_0:
                    pe.wait_ge(h1_copied, M1 * s + m - L1_0 + 1)
                elif m < L3_0:
                    pe.wait_ge(h2_copied, M2 * s + m - L2_0 + 1)
                else:
                    pe.wait_ge(y_copied, s + 1)

            def turn(s, first, t):
                for k in range(QUADS):
                    n = QUADS * t + k
                    if not (first and n < 2):
                        pe.wait_ge(turned_copied, T * QUADS * s + n - 1)
                    pe.wait_ge(rows_in[t % 2][k], 16 * len(looked_up[k]) * (T // 2 * s + t // 2 + 1))
                    if k == QUADS - 1:
                        pe.wait_ge(dense_in, 16 * s + 16)
                    for j, f in enumerate(quad[k]):
                        src = rows[t % 2][:, f, :] if f < F else dense_sb[:, t, :]
                        last = pe.transpose(tp[n % 2][:, j, :], src, ident[:, :])
                    last.then_inc(turned, 1)

            def gram(s, first, t):
                pe.wait_ge(turned_copied, T * QUADS * s + QUADS * (t + 1))
                for j in range(GFILLS):
                    n = GFILLS * t + j
                    if not (first and n < 2):
                        pe.wait_ge(gram_copied, T * GFILLS * s + n - 1)
                    for g in range(FG):
                        p0 = GS * (FG * j + g)
                        out = gm[n % 2][:, g, 0:GS * ITEMS].rearrange("p (c f) -> p c f", c=GS)
                        last = pe.matmul(out, eT[t % 2][:, p0:p0 + GS, :].rearrange("p c f -> p (c f)"),
                                         eT[t % 2][:, p0:p0 + GS, 0:ITEMS], start=True, stop=True)
                    last.then_inc(gram_done, 1)

            def tower(s, first):
                pe.wait_ge(gram_copied, T * GFILLS * (s + 1))
                for u in range(UFILLS):
                    shared_bank_free(s, first, U0 + u)
                    for j, g in enumerate(gcols[UQ * u:UQ * u + UQ]):
                        last = pe.transpose(mx[(U0 + u) % 2][:, P * j:P * j + P], gramZ[:, g, :], ident[:, :])
                    last.then_inc(regrouped, 1)
                pe.wait_ge(feats_copied, UFILLS * (s + 1))
                for k in range(ZC):
                    shared_bank_free(s, first, V0 + k)
                    for c in range(GS):
                        last = pe.transpose(mx[(V0 + k) % 2][0:ZK, P * c:P * c + P],
                                            feats[:, c, ZK * k:ZK * k + ZK], ident[:, :])
                    last.then_inc(feats_turned, 1)
                if first:
                    pe.wait_ge(w1_in, 16)
                    pe.wait_ge(w1s_ok, 1)
                    pe.wait_ge(tail_in, 64)
                for m in range(M1):
                    shared_bank_free(s, first, L1_0 + m)
                    acc = mx[(L1_0 + m) % 2][:, :]
                    pe.matmul(acc, w1s[:, P * m:P * m + P], dT[:, :, :, :].rearrange("p c t i -> p (c t i)"),
                              start=True, stop=False)
                    for k in range(ZC):
                        if m == 0:
                            pe.wait_ge(featsT_copied, ZC * s + k + 1)
                        last = pe.matmul(acc, w1[:, k, P * m:P * m + P], featsT[:, k, :],
                                         start=False, stop=(k == ZC - 1))
                    last.then_inc(h1_done, 1)
                for m in range(M2):
                    shared_bank_free(s, first, L2_0 + m)
                    acc = mx[(L2_0 + m) % 2][:, :]
                    for k in range(M1):
                        if m == 0:
                            pe.wait_ge(h1_copied, M1 * s + k + 1)
                        last = pe.matmul(acc, w2[:, k, P * m:P * m + P], h1T[:, k, :],
                                         start=(k == 0), stop=(k == M1 - 1))
                    last.then_inc(h2_done, 1)
                shared_bank_free(s, first, L3_0)
                pe.wait_ge(h2_copied, M2 * (s + 1))
                for c in range(GS):
                    for k in range(M2):
                        last = pe.matmul(mx[L3_0 % 2][:, c:c + 1], h2T[:, k, P * c:P * c + P], w3[:, k:k + 1],
                                         start=(k == 0), stop=(k == M2 - 1))
                last.then_inc(y_done, 1)

            def whole_block(s, first):
                for t in range(T):
                    turn(s, first, t)
                    gram(s, first, t)
                tower(s, first)

            pe.wait_ge(ident_ok, 1)
            pe.wait_ge(slots_zero, 1)
            blocks(pe, whole_block)

        @block.scalar
        def _(act):
            def items_out(s, t):
                for k in range(QUADS):
                    n = QUADS * t + k
                    act.wait_ge(turned, T * QUADS * s + n + 1)
                    f0, m = quad[k][0], len(quad[k])
                    if k == QUADS - 1:
                        act.activation(dT[:, :, t, :].rearrange("p c i -> p i c"),
                                       tp[n % 2][:, m - 1, :].rearrange("p (i c) -> p i c", c=GS), ACT.Copy)
                    act.activation(eT[t % 2][:, :, f0:f0 + m].rearrange("p b f -> p f b"),
                                   tp[n % 2][:, 0:m, :], ACT.Copy).then_inc(turned_copied, 1)

            def tower_out(s, first):
                for k in range(ZC):
                    act.wait_ge(feats_turned, ZC * s + k + 1)
                    act.activation(featsT[:, k, :], mx[(V0 + k) % 2][0:ZK, :], ACT.Copy).then_inc(featsT_copied, 1)
                if first:
                    act.wait_ge(tail_in, 64)
                for m in range(M1):
                    act.wait_ge(h1_done, M1 * s + m + 1)
                    act.activation(h1T[:, m, :], mx[(L1_0 + m) % 2][:, :], ACT.Relu,
                                   bias=b1[:, m:m + 1]).then_inc(h1_copied, 1)
                for m in range(M2):
                    act.wait_ge(h2_done, M2 * s + m + 1)
                    act.activation(h2T[:, m, :], mx[(L2_0 + m) % 2][:, :], ACT.Relu,
                                   bias=b2[:, m:m + 1]).then_inc(h2_copied, 1)
                act.wait_ge(y_copied, s + 1)
                act.dma_start(y[bass.ds(BS * s, BS), :].rearrange("(i c) n -> i (c n)", c=GS),
                              y_sb[:, :]).then_inc(y_out, 16)

            def whole_block(s, first):
                for t in range(T):
                    items_out(s, t)
                tower_out(s, first)

            act.wait_ge(slots_zero, 1)
            blocks(act, whole_block)

        @block.vector
        def _(dve):
            for j in range(2):
                last = dve.memset(eT[j][:, :, ITEMS:SLOT], 0.0)
            last.then_inc(slots_zero, 1)
            dve.wait_ge(w1d_in, 32)
            dve.tensor_tensor(w1s[:, :], w1d[:, 0, :], w1d[:, 1, :], ALU.add).then_inc(w1s_ok, 1)

            def grams_out(s, t):
                for j in range(GFILLS):
                    n = GFILLS * t + j
                    dve.wait_ge(gram_done, T * GFILLS * s + n + 1)
                    i0 = GT * t + FG * j
                    for c in range(GS):
                        q = slice(SLOT * c, SLOT * c + SLOT)
                        last = dve.tensor_copy(gramZ[q, :, i0:i0 + FG].rearrange("p g i -> p i g"),
                                               gm[n % 2][q, :, ITEMS * c:ITEMS * c + ITEMS])
                    last.then_inc(gram_copied, 1)

            def feats_out(s):
                for u in range(UFILLS):
                    dve.wait_ge(regrouped, UFILLS * s + u + 1)
                    for j, g in enumerate(gcols[UQ * u:UQ * u + UQ]):
                        bank = mx[(U0 + u) % 2][:, P * j:P * j + P].rearrange("p (c f) -> p c f", c=GS)
                        if g == F:
                            last = dve.tensor_copy(feats[:, :, 0:F], bank[:, :, 0:F])
                        else:
                            m = F - 1 - g
                            last = dve.tensor_copy(feats[:, :, pair_row[g]:pair_row[g] + m],
                                                   bank[:, :, g + 1:F])
                    last.then_inc(feats_copied, 1)

            def whole_block(s, first):
                for t in range(T):
                    grams_out(s, t)
                feats_out(s)
                if not first:
                    dve.wait_ge(y_out, 16 * s)
                dve.wait_ge(y_done, s + 1)
                dve.tensor_copy(y_sb[:, :], mx[L3_0 % 2][:, 0:GS]).then_inc(y_copied, 1)

            blocks(dve, whole_block)


def kernel(**inputs):
    import numpy as _np
    import concourse.bacc as _bacc
    from concourse import mybir as _mybir
    from concourse.bass_utils import run_bass_kernel_spmd as _run

    nc = _bacc.Bacc("TRN2", target_bir_lowering=False, num_devices=1)
    arrays, aps = {}, {}
    for name in inputs:
        a = _np.ascontiguousarray(inputs[name])
        arrays[f"in_{name}_dram"] = a
        aps[name] = nc.dram_tensor(f"in_{name}_dram", a.shape, _mybir.dt.from_np(a.dtype), kind="ExternalInput").ap()
    n_tables = aps["ids"].shape[1]
    y = nc.dram_tensor("out_0_dram", (aps["ids"].shape[0], 1), _mybir.dt.float32, kind="ExternalOutput").ap()
    dlrm_tower_kernel(nc, aps["r_dense_features"], aps["ids"], [aps[f"tbl_{f}"] for f in range(n_tables)],
                      aps["W_top1"], aps["b_top1"], aps["W_top2"], aps["b_top2"], aps["W_top3"], y)
    r = _run(nc, [arrays], core_ids=[0])
    return r.results[0]["out_0_dram"]
```

```python
import concourse.bass as bass
from concourse import mybir
from contextlib import ExitStack


def dlrm_tower_kernel(nc, dense, ids, tables, W_top1, b_top1, W_top2, b_top2, W_top3, y):
    fp32 = mybir.dt.float32
    fp32r = mybir.dt.float32r
    fp16 = mybir.dt.float16
    int32 = mybir.dt.int32
    ALU = mybir.AluOpType
    ACT = mybir.ActivationFunctionType

    P = 128
    B, D = dense.shape
    F = len(tables)
    ITEMS = F + 1
    N1, N2 = W_top1.shape[1], W_top2.shape[1]
    BS = 512
    S = B // BS
    T = BS // P
    GS = 4
    SLOT = P // GS
    GT = P // GS
    FG = 4
    GFILLS = GT // FG
    FEATS_PARTS = 3
    FEATS_AFTER = 5

    MATMUL_TABLES = (12, 13, 14, 15, 17, 18, 20)[:6]
    L = len(MATMUL_TABLES)
    V = tables[MATMUL_TABLES[0]].shape[0]
    VC = -(-V // P)
    VP = V // VC
    assert VC * VP == V and V <= 2048 and all(tables[f].shape[0] == V for f in MATMUL_TABLES)

    QUAD = 4
    gathered = [f for f in range(F) if f not in MATMUL_TABLES]
    turned_items = gathered + [F]
    QUADS = -(-len(turned_items) // QUAD)
    TF = T * QUADS
    quad = [turned_items[QUAD * k:QUAD * k + QUAD] for k in range(QUADS)]
    assert TF % 2 == 0

    def runs(items):
        out = []
        for j, f in enumerate(items):
            if out and out[-1][1] + out[-1][2] == f:
                out[-1][2] += 1
            else:
                out.append([j, f, 1])
        return out

    PAIRS = F * (F - 1) // 2
    Z = F + PAIRS
    ZC = 3
    ZK = Z // ZC
    assert ZC * ZK == Z and ZK <= P
    pair_at = [F + f * (F - 1) - f * (f - 1) // 2 for f in range(F)]
    M1, M2 = N1 // P, N2 // P

    FEATS, H1, H2, Y = range(4)
    SHARED = [(FEATS, t) for t in range(T)] + [(H1, m) for m in range(M1)] + [(H2, m) for m in range(M2)] + [(Y, 0)]
    TAIL = SHARED[:T - 1] + SHARED[T:] + [(FEATS, T - 1)] + SHARED[T:]

    ctx = ExitStack()
    with ctx:
        def sb(name, shape, dt=fp32):
            return ctx.enter_context(nc.sbuf_tensor(name, shape, dt))

        def pb(name, shape):
            return ctx.enter_context(nc.psum_tensor(name, shape, fp32))

        def sem(name):
            return ctx.enter_context(nc.semaphore(name))

        ids_sb = sb("ids_sb", [P, T, F], int32)
        ids_mm = sb("ids_mm", [P, T, F], int32)
        ids16 = sb("ids16", [P, T, F], fp16)
        rows = [sb(f"rows{j}", [P, len(gathered), D]) for j in range(2)]
        dense_sb = sb("dense_sb", [P, T, D])
        eT = sb("eT", [P, T, GT, GS, SLOT])
        dT = sb("dT", [P, BS])
        table_hi = sb("table_hi", [VP, L, VC, D], fp32r)
        table_lo = sb("table_lo", [VP, L, VC, D], fp32r)
        row_of = sb("row_of", [VP, VC])
        onehot = sb("onehot", [VP, VC, BS], fp32r)
        gram_sb = [sb(f"gram_sb{j}", [P, ITEMS, GT]) for j in range(2)]
        gram_i = sb("gram_i", [P, ITEMS, SLOT])
        feats = [sb(f"feats{j}", [P, Z]) for j in range(2)]
        featsT = sb("featsT", [ZK, ZC, BS])
        h1T = sb("h1T", [P, M1, BS])
        h2T = sb("h2T", [P, M2, BS])
        y_sb = sb("y_sb", [P, T])
        w1 = sb("w1", [ZK, ZC, N1])
        w1s = sb("w1s", [P, N1])
        w2 = sb("w2", [P, M1, N2])
        w3 = sb("w3", [P, M2])
        b1 = sb("b1", [P, M1])
        b2 = sb("b2", [P, M2])
        ident = sb("ident", [P, P])
        ident16 = sb("ident16", [P, P], fp16)
        RAW = M1 * BS // (VC * D)
        raw_table = h1T[:, :, :].rearrange("p m b -> p (m b)").rearrange("p (j c d) -> p j c d", j=RAW, c=VC)
        w1d = h2T[:, :, :]

        tp = [pb(f"tp{j}", [P, QUAD, P]) for j in range(2)]
        gm = [pb(f"gm{j}", [P, FG, P]) for j in range(2)]
        mx = [pb(f"mx{j}", [P, BS]) for j in range(2)]
        idb = pb("idb", [P, BS])
        looked = pb("looked", [P, BS])

        ids_in = [sem(f"ids_in{t}") for t in range(T)]
        ids_mm_in = sem("ids_mm_in")
        dense_in = [sem(f"dense_in{t}") for t in range(T)]
        table_in = [sem(f"table_in{j}") for j in range(RAW)]
        w1_in = sem("w1_in")
        w1d_in = sem("w1d_in")
        tail_in = sem("tail_in")
        y_out = sem("y_out")
        rows_in = [[sem(f"rows_in{j}_{k}") for k in range(QUADS)] for j in range(2)]
        pool_steps = sem("pool_steps")
        ident_zero = sem("ident_zero")
        ident_ok = sem("ident_ok")
        row_of_ok = sem("row_of_ok")
        ident16_ok = sem("ident16_ok")
        slots_zero = sem("slots_zero")
        w1s_ok = sem("w1s_ok")
        hi_ok = sem("hi_ok")
        lo_ok = sem("lo_ok")
        ids16_ok = sem("ids16_ok")
        ids_spread = sem("ids_spread")
        onehot_ok = sem("onehot_ok")
        onehot_used = sem("onehot_used")
        looked_copied = sem("looked_copied")
        turned = sem("turned")
        turned_copied = sem("turned_copied")
        gram_done = sem("gram_done")
        gram_copied = sem("gram_copied")
        gram01_copied = sem("gram01_copied")
        gram_turned = sem("gram_turned")
        feats_ok = sem("feats_ok")
        feats_turned = sem("feats_turned")
        featsT_copied = sem("featsT_copied")
        h1_done = sem("h1_done")
        h1_copied = sem("h1_copied")
        h2_done = sem("h2_done")
        h2_copied = sem("h2_copied")
        y_done = sem("y_done")
        y_copied = sem("y_copied")

        block = ctx.enter_context(nc.Block())

        def blocks(eng, body):
            body(0, True, False)
            with eng.Fori(1, S - 1) as s:
                body(s, False, False)
            body(S - 1, False, True)

        @block.sync
        def _(sp):
            ids_t = ids.rearrange("(s p t) f -> s p t f", p=P, t=T)
            dense_t = dense.rearrange("(s p t) d -> s p t d", p=P, t=T)
            table_t = [tables[f].rearrange("(p c) d -> p c d", c=VC) for f in MATMUL_TABLES]
            for t in range(T):
                sp.dma_start(ids_sb[:, t, :], ids_t[0, :, t, :]).then_inc(ids_in[t], 16)
            sp.dma_start(ids_mm[:, :, :], ids_t[0]).then_inc(ids_mm_in, 16)
            for j in range(L):
                if j >= RAW:
                    sp.wait_ge(hi_ok, j - RAW + 1)
                    sp.wait_ge(lo_ok, j - RAW + 1)
                sp.dma_start(raw_table[0:VP, j % RAW], table_t[j]).then_inc(table_in[j % RAW], 16)
                if j == 1:
                    for t in range(T):
                        sp.dma_start(dense_sb[:, t, :], dense_t[0, :, t, :]).then_inc(dense_in[t], 16)
                    sp.dma_start(w1d[:, 0, :], W_top1[0:D, :]).then_inc(w1d_in, 16)
                    sp.dma_start(w1d[:, 1, :], W_top1[D + Z:D + Z + D, :]).then_inc(w1d_in, 16)
            sp.dma_start(w1[:, :, :], W_top1[D:D + Z, :].rearrange("(k p) n -> p k n", p=ZK)).then_inc(w1_in, 16)
            sp.dma_start(w2[:, :, :], W_top2.rearrange("(k p) n -> p k n", p=P)).then_inc(tail_in, 16)
            with nc.allow_non_contiguous_dma(reason="a few hundred words, once"):
                sp.dma_start(w3[:, :], W_top3.rearrange("(k p) n -> p (k n)", p=P)).then_inc(tail_in, 16)
                sp.dma_start(b1[:, :], b_top1.rearrange("(k p) -> p k", p=P)).then_inc(tail_in, 16)
                sp.dma_start(b2[:, :], b_top2.rearrange("(k p) -> p k", p=P)).then_inc(tail_in, 16)
            with sp.Fori(1, S) as s:
                sp.wait_ge(ids16_ok, s)
                sp.dma_start(ids_mm[:, :, :],
                             ids[bass.ds(BS * s, BS), :].rearrange("(p t) f -> p t f", t=T)).then_inc(ids_mm_in, 16)
                for t in range(T):
                    sp.wait_ge(turned, TF * (s - 1) + QUADS * (t + 1))
                    sp.dma_start(ids_sb[:, t, :], ids[bass.ds(BS * s, BS), :].rearrange(
                        "(p t) f -> p t f", t=T)[:, t, :]).then_inc(ids_in[t], 16)
                    sp.dma_start(dense_sb[:, t, :], dense[bass.ds(BS * s, BS), :].rearrange(
                        "(p t) d -> p t d", t=T)[:, t, :]).then_inc(dense_in[t], 16)
            sp.wait_ge(y_out, 16 * S)

        @block.gpsimd
        def _(pool):
            pool.iota(row_of[:, :], pattern=[[1, VC]], base=0, channel_multiplier=VC,
                      allow_small_or_imprecise_dtypes=True).then_inc(row_of_ok, 1)
            pool.memset(ident[:, :], 0.0).then_inc(ident_zero, 1)
            pool.wait_ge(ident_zero, 1)
            pool.affine_select(out=ident[:, :], in_=ident[:, :], compare_op=ALU.not_equal, fill=1.0,
                               base=0, pattern=[[-1, P]], channel_multiplier=1).then_inc(ident_ok, 1)

            def gathers(s, first):
                for t in range(T):
                    pool.wait_ge(ids_in[t], 16 * s + 16)
                    pool.sem_inc(pool_steps, 1)
                    for k in range(QUADS):
                        if not (first and t < 2):
                            pool.wait_ge(turned, TF * s + QUADS * (t - 2) + k + 1)
                            pool.sem_inc(pool_steps, 1)
                        for f in quad[k]:
                            if f < F:
                                pool.indirect_dma_start(
                                    rows[t % 2][:, gathered.index(f), :], None, tables[f],
                                    bass.IndirectOffsetOnAxis(ids_sb[:, t, f:f + 1], 0)
                                ).then_inc(rows_in[t % 2][k], 16)

            gathers(0, True)
            with pool.Fori(1, S) as s:
                gathers(s, False)

        @block.tensor
        def _(pe):
            def shared_bank(s, first, last, n):
                fills = TAIL if last else SHARED
                m, of = n - 2, s
                if m < 0:
                    if first:
                        return mx[n % 2]
                    m, of, fills = len(SHARED) - 1 - (len(SHARED) - 1 - n) % 2, s - 1, SHARED
                kind, j = fills[m]
                q = S if fills is TAIL and m > T - 1 + M1 + M2 else of
                if kind == FEATS:
                    pe.wait_ge(featsT_copied, T * of + j + 1)
                elif kind == H1:
                    pe.wait_ge(h1_copied, M1 * q + j + 1)
                elif kind == H2:
                    pe.wait_ge(h2_copied, M2 * q + j + 1)
                else:
                    pe.wait_ge(y_copied, q + 1)
                return mx[n % 2]

            def spread_ids(s, j):
                f = MATMUL_TABLES[j]
                pe.wait_ge(ids16_ok, s + 1)
                if not (isinstance(s, int) and s == 0 and j == 0):
                    pe.wait_ge(onehot_ok, VC * (L * s + j))
                for t in range(T):
                    last_mm = pe.matmul(idb[:, P * t:P * t + P], ids16[:, t, f:f + 1].to_broadcast([P, P]),
                                        ident16[:, :], start=True, stop=True)
                last_mm.then_inc(ids_spread, 1)

            def look_up(s, j):
                if j + 1 < L:
                    spread_ids(s, j + 1)
                if isinstance(s, int) and s == 0:
                    pe.wait_ge(hi_ok, j + 1)
                    pe.wait_ge(lo_ok, j + 1)
                if not (isinstance(s, int) and s == 0 and j == 0):
                    pe.wait_ge(looked_copied, L * s + j)
                for c in range(VC):
                    pe.wait_ge(onehot_ok, VC * (L * s + j) + c + 1)
                    pe.matmul(looked[:, :], table_hi[:, j, c, :], onehot[:, c, :], start=(c == 0), stop=False)
                    pe.matmul(looked[:, :], table_lo[:, j, c, :], onehot[:, c, :],
                              start=False, stop=(c == VC - 1)).then_inc(onehot_used, 1)

            def turn(s, first, t, k):
                n = QUADS * t + k
                if not (first and n < 2):
                    pe.wait_ge(turned_copied, TF * s + n - 1)
                pe.wait_ge(rows_in[t % 2][k], 16 * sum(f < F for f in quad[k]) * (T // 2 * s + t // 2 + 1))
                if k == QUADS - 1:
                    pe.wait_ge(dense_in[t], 16 * s + 16)
                for j, f in enumerate(quad[k]):
                    src = rows[t % 2][:, gathered.index(f), :] if f < F else dense_sb[:, t, :]
                    last_mm = pe.transpose(tp[n % 2][:, j, :], src, ident[:, :])
                last_mm.then_inc(turned, 1)

            def gram(s, first, t, turning, bank=None):
                pe.wait_ge(turned_copied, TF * s + QUADS * (t + 1))
                if t == 0:
                    pe.wait_ge(looked_copied, L * (s + 1))
                for j in range(GFILLS):
                    n = GFILLS * t + j
                    if not (first and n < 2):
                        pe.wait_ge(gram_copied, T * GFILLS * s + n - 1)
                        pe.wait_ge(gram01_copied, T * GFILLS * s + n - 1)
                    for g in range(FG):
                        i = FG * j + g
                        out = gm[n % 2][:, g, 0:GS * ITEMS].rearrange("p (c f) -> p c f", c=GS)
                        last_mm = pe.matmul(out, eT[:, t, i, :, :].rearrange("p c f -> p (c f)"), eT[:, t, i, :, 0:ITEMS],
                                            start=True, stop=True)
                    last_mm.then_inc(gram_done, 1)
                    if turning and j >= 1 and j - 1 < QUADS:
                        turn(s, first, t + 1, j - 1)
                    if bank and j == FEATS_AFTER:
                        turn_feats(s, t - 1, bank())

            def turn_feats(s, t, bank):
                pe.wait_ge(feats_ok, T * s + t + 1)
                for k in range(ZC):
                    last_mm = pe.transpose(bank[0:ZK, P * k:P * k + P], feats[t % 2][:, ZK * k:ZK * k + ZK],
                                           ident[:, :])
                last_mm.then_inc(feats_turned, 1)

            def layer1(s, m, t0, t1, bank):
                cols = slice(P * t0, P * t1)
                acc = bank[:, 0:P * (t1 - t0)]
                if m == 0:
                    pe.wait_ge(featsT_copied, T * s + t1)
                pe.matmul(acc, w1s[:, P * m:P * m + P], dT[:, cols], start=True, stop=False)
                for k in range(ZC):
                    last_mm = pe.matmul(acc, w1[:, k, P * m:P * m + P], featsT[:, k, cols],
                                        start=False, stop=(k == ZC - 1))
                last_mm.then_inc(h1_done, 1)

            def layer2(q, m, t0, t1, bank):
                acc = bank[:, 0:P * (t1 - t0)]
                for k in range(M1):
                    if m == 0:
                        pe.wait_ge(h1_copied, M1 * q + k + 1)
                    last_mm = pe.matmul(acc, w2[:, k, P * m:P * m + P], h1T[:, k, P * t0:P * t1],
                                        start=(k == 0), stop=(k == M1 - 1))
                last_mm.then_inc(h2_done, 1)

            def layer3(q, t0, t1, bank):
                pe.wait_ge(h2_copied, M2 * (q + 1))
                for t in range(t0, t1):
                    for k in range(M2):
                        last_mm = pe.matmul(bank[:, t:t + 1], h2T[:, k, P * t:P * t + P], w3[:, k:k + 1],
                                            start=(k == 0), stop=(k == M2 - 1))
                last_mm.then_inc(y_done, 1)

            def whole_block(s, first, last):
                fill = [0]

                def bank():
                    fill[0] += 1
                    return shared_bank(s, first, last, fill[0] - 1)

                gram(s, first, 0, True)
                if not last:
                    spread_ids(s + 1, 0)
                gram(s, first, 1, True, bank)
                gram(s, first, 2, not last, bank)
                if last:
                    turn_feats(s, 2, bank())
                    for m in range(M1):
                        layer1(s, m, 0, 3, bank())
                    for k in range(QUADS):
                        turn(s, first, 3, k)
                    gram(s, first, 3, False)
                    for m in range(M2):
                        layer2(s, m, 0, 3, bank())
                    layer3(s, 0, 3, bank())
                    turn_feats(s, 3, bank())
                    for m in range(M1):
                        layer1(s, m, 3, 4, bank())
                    for m in range(M2):
                        layer2(S, m, 3, 4, bank())
                    layer3(S, 3, 4, bank())
                else:
                    gram(s, first, 3, False, bank)
                    look_up(s + 1, 0)
                    turn_feats(s, 3, bank())
                    for m in range(M1):
                        layer1(s, m, 0, T, bank())
                        if m == 1:
                            look_up(s + 1, 1)
                        elif m > 1:
                            turn(s + 1, False, 0, 2 * m - 4)
                            turn(s + 1, False, 0, 2 * m - 3)
                    look_up(s + 1, 2)
                    for k in range(4, QUADS):
                        turn(s + 1, False, 0, k)
                    for m in range(M2):
                        layer2(s, m, 0, T, bank())
                        look_up(s + 1, 3 + m)
                    layer3(s, 0, T, bank())
                    for j in range(3 + M2, L):
                        look_up(s + 1, j)

            pe.wait_ge(ident16_ok, 1)
            spread_ids(0, 0)
            for j in range(L):
                look_up(0, j)
            pe.wait_ge(ident_ok, 1)
            for k in range(QUADS):
                turn(0, True, 0, k)
            pe.wait_ge(slots_zero, 1)
            pe.wait_ge(w1_in, 16)
            pe.wait_ge(w1s_ok, 1)
            pe.wait_ge(tail_in, 64)
            blocks(pe, whole_block)

        @block.scalar
        def _(act):
            def looked_out(s, j):
                act.wait_ge(onehot_used, VC * (L * s + j + 1))
                f = MATMUL_TABLES[j]
                act.activation(eT[:, :, :, :, f].rearrange("p t i c -> p t c i"),
                               looked[:, :].rearrange("p (t c i) -> p t c i", t=T, c=GS),
                               ACT.Copy).then_inc(looked_copied, 1)

            def items_out(s, t, k):
                n = QUADS * t + k
                act.wait_ge(turned, TF * s + n + 1)
                if k == QUADS - 1:
                    act.activation(dT[:, P * t:P * t + P], tp[n % 2][:, len(quad[k]) - 1, :], ACT.Copy)
                for j, f, m in runs(quad[k]):
                    last_copy = act.activation(
                        eT[:, t, :, :, f:f + m].rearrange("p i c f -> p f c i"),
                        tp[n % 2][:, j:j + m, :].rearrange("p f (c i) -> p f c i", c=GS), ACT.Copy)
                last_copy.then_inc(turned_copied, 1)

            def quadrant_out(t, j, n, c):
                q = slice(SLOT * c, SLOT * c + SLOT)
                return act.activation(gram_sb[t % 2][q, :, FG * j:FG * j + FG].rearrange("p g i -> p i g"),
                                      gm[n % 2][q, :, ITEMS * c:ITEMS * c + ITEMS], ACT.Copy)

            def gram01_out(s, first, t, turning, next_fill=None):
                for j in range(GFILLS):
                    n = GFILLS * t + j
                    act.wait_ge(gram_done, T * GFILLS * s + n + 1)
                    if j == 0 and not (first and t < 2):
                        act.wait_ge(gram_turned, T * s + t - 1)
                    quadrant_out(t, j, n, 0)
                    quadrant_out(t, j, n, 1).then_inc(gram01_copied, 1)
                    if turning and j >= 1 and j - 1 < QUADS:
                        items_out(s, t + 1, j - 1)
                    if next_fill and j == FEATS_AFTER:
                        feats_out(s, next_fill(), t - 1)

            def feats_out(s, n_shared, t):
                act.wait_ge(feats_turned, T * s + t + 1)
                act.activation(featsT[:, :, P * t:P * t + P],
                               mx[n_shared % 2][0:ZK, 0:ZC * P].rearrange("p (k b) -> p k b", k=ZC),
                               ACT.Copy).then_inc(featsT_copied, 1)

            def h1_out(q, m, t0, t1, n_shared):
                act.wait_ge(h1_done, M1 * q + m + 1)
                act.activation(h1T[:, m, P * t0:P * t1], mx[n_shared % 2][:, 0:P * (t1 - t0)], ACT.Relu,
                               bias=b1[:, m:m + 1]).then_inc(h1_copied, 1)

            def h2_out(q, m, t0, t1, n_shared):
                act.wait_ge(h2_done, M2 * q + m + 1)
                act.activation(h2T[:, m, P * t0:P * t1], mx[n_shared % 2][:, 0:P * (t1 - t0)], ACT.Relu,
                               bias=b2[:, m:m + 1]).then_inc(h2_copied, 1)

            def whole_block(s, first, last):
                fill = [0]

                def next_fill():
                    fill[0] += 1
                    return fill[0] - 1

                gram01_out(s, first, 0, True)
                gram01_out(s, first, 1, True, next_fill)
                gram01_out(s, first, 2, not last, next_fill)
                if last:
                    feats_out(s, next_fill(), 2)
                    for m in range(M1):
                        h1_out(s, m, 0, 3, next_fill())
                    for k in range(QUADS):
                        items_out(s, 3, k)
                    gram01_out(s, first, 3, False)
                    for m in range(M2):
                        h2_out(s, m, 0, 3, next_fill())
                    next_fill()
                    feats_out(s, next_fill(), 3)
                    for m in range(M1):
                        h1_out(S, m, 3, 4, next_fill())
                    for m in range(M2):
                        h2_out(S, m, 3, 4, next_fill())
                else:
                    gram01_out(s, first, 3, False, next_fill)
                    looked_out(s + 1, 0)
                    feats_out(s, next_fill(), 3)
                    for m in range(M1):
                        h1_out(s, m, 0, T, next_fill())
                        if m == 1:
                            looked_out(s + 1, 1)
                        elif m > 1:
                            items_out(s + 1, 0, 2 * m - 4)
                            items_out(s + 1, 0, 2 * m - 3)
                    looked_out(s + 1, 2)
                    for k in range(4, QUADS):
                        items_out(s + 1, 0, k)
                    for m in range(M2):
                        h2_out(s, m, 0, T, next_fill())
                        looked_out(s + 1, 3 + m)
                    for j in range(3 + M2, L):
                        looked_out(s + 1, j)
                act.wait_ge(y_copied, S + 1 if last else s + 1)
                act.dma_start(y[bass.ds(BS * s, BS), :].rearrange("(p t) n -> p (t n)", t=T),
                              y_sb[:, :]).then_inc(y_out, 16)

            for j in range(L):
                act.wait_ge(table_in[j % RAW], 16 * (j // RAW + 1))
                act.activation(table_hi[:, j, :, :], raw_table[0:VP, j % RAW], ACT.Copy).then_inc(hi_ok, 1)
                if j >= 1:
                    looked_out(0, j - 1)
            looked_out(0, L - 1)
            for k in range(QUADS):
                items_out(0, 0, k)
            act.wait_ge(tail_in, 64)
            blocks(act, whole_block)

        @block.vector
        def _(dve):
            def convert_ids(s):
                dve.wait_ge(ids_mm_in, 16 * s + 16)
                if not (isinstance(s, int) and s == 0):
                    dve.wait_ge(ids_spread, L * s)
                for j, f, m in runs(MATMUL_TABLES):
                    last_op = dve.tensor_copy(ids16[:, :, f:f + m], ids_mm[:, :, f:f + m])
                last_op.then_inc(ids16_ok, 1)

            def compare_ids(s, j, chunks=range(VC)):
                dve.wait_ge(ids_spread, L * s + j + 1)
                for c in chunks:
                    if not (isinstance(s, int) and s == 0 and j == 0):
                        dve.wait_ge(onehot_used, VC * (L * s + j - 1) + c + 1)
                    dve.tensor_scalar(onehot[:, c, :], idb[0:VP, :], row_of[:, c:c + 1], None,
                                      ALU.is_equal).then_inc(onehot_ok, 1)

            def grams_out(s, first, t, last):
                for j in range(GFILLS):
                    n = GFILLS * t + j
                    dve.wait_ge(gram_done, T * GFILLS * s + n + 1)
                    for c in range(2, GS):
                        q = slice(SLOT * c, SLOT * c + SLOT)
                        last_op = dve.tensor_copy(
                            gram_sb[t % 2][q, :, FG * j:FG * j + FG].rearrange("p g i -> p i g"),
                            gm[n % 2][q, :, ITEMS * c:ITEMS * c + ITEMS])
                    last_op.then_inc(gram_copied, 1)
                    if t == 0 or (last and t == T - 1):
                        continue
                    if j == 0:
                        gram_turn(s, first, t - 1)
                    elif j <= FEATS_PARTS:
                        feats_out(s, first, t - 1, j - 1)
                    elif t < T - 1 and not last:
                        spare = GFILLS - 1 - FEATS_PARTS
                        step, steps = spare * (t - 1) + j - 1 - FEATS_PARTS, spare * (T - 2)
                        compare_ids(s + 1, 0, range(VC * step // steps, VC * (step + 1) // steps))

            def gram_turn(s, first, t):
                dve.wait_ge(gram_copied, T * GFILLS * s + GFILLS * (t + 1))
                dve.wait_ge(gram01_copied, T * GFILLS * s + GFILLS * (t + 1))
                if not (first and t == 0):
                    dve.wait_ge(feats_ok, T * s + t)
                dve.transpose(gram_i[:, :, :].rearrange("p g f -> p (g f)"),
                              gram_sb[t % 2][:, :, :].rearrange("p g i -> p (g i)")).then_inc(gram_turned, 1)

            def feats_out(s, first, t, part):
                if part == 0:
                    dve.wait_ge(gram_turned, T * s + t + 1)
                    if not (first and t < 2):
                        dve.wait_ge(feats_turned, T * s + t - 1)
                z = feats[t % 2]
                for f in range(F * part // FEATS_PARTS, F * (part + 1) // FEATS_PARTS):
                    if f == F - 1:
                        last_op = dve.tensor_copy(z[:, 0:F], gram_i[:, F, 0:F])
                    else:
                        last_op = dve.tensor_copy(z[:, pair_at[f]:pair_at[f] + F - 1 - f], gram_i[:, f, f + 1:F])
                if part == FEATS_PARTS - 1:
                    last_op.then_inc(feats_ok, 1)

            def y_copy(q, t0, t1, n_shared):
                dve.wait_ge(y_done, q + 1)
                dve.tensor_copy(y_sb[:, t0:t1], mx[n_shared % 2][:, t0:t1]).then_inc(y_copied, 1)

            def whole_block(s, first, last):
                for t in range(T):
                    grams_out(s, first, t, last)
                    if not last and t == 0:
                        convert_ids(s + 1)
                    if t == T - 1 or (last and t == T - 2):
                        gram_turn(s, first, t)
                        for part in range(FEATS_PARTS):
                            feats_out(s, first, t, part)
                if last:
                    dve.wait_ge(y_out, 16 * s)
                    y_copy(s, 0, T - 1, T - 1 + M1 + M2)
                    y_copy(S, T - 1, T, len(TAIL) - 1)
                else:
                    for j in range(1, L):
                        compare_ids(s + 1, j)
                    if not first:
                        dve.wait_ge(y_out, 16 * s)
                    y_copy(s, 0, T, len(SHARED) - 1)

            dve.memset(eT[:, :, :, :, ITEMS:SLOT].rearrange("p t i c f -> p (t i c) f"), 0.0).then_inc(slots_zero, 1)
            dve.wait_ge(ident_ok, 1)
            dve.tensor_copy(ident16[:, :], ident[:, :]).then_inc(ident16_ok, 1)
            convert_ids(0)
            dve.wait_ge(row_of_ok, 1)
            for j in range(L):
                dve.wait_ge(hi_ok, j + 1)
                dve.tensor_tensor(table_lo[:, j, :, :], raw_table[0:VP, j % RAW], table_hi[:, j, :, :].bitcast(fp32),
                                  ALU.subtract).then_inc(lo_ok, 1)
                compare_ids(0, j)
            dve.wait_ge(w1d_in, 32)
            dve.tensor_tensor(w1s[:, :], w1d[:, 0, :], w1d[:, 1, :], ALU.add).then_inc(w1s_ok, 1)
            blocks(dve, whole_block)


def kernel(**inputs):
    import numpy as _np
    import concourse.bacc as _bacc
    from concourse import mybir as _mybir
    from concourse.bass_utils import run_bass_kernel_spmd as _run

    nc = _bacc.Bacc("TRN2", target_bir_lowering=False, num_devices=1)
    arrays, aps = {}, {}
    for name in inputs:
        a = _np.ascontiguousarray(inputs[name])
        arrays[f"in_{name}_dram"] = a
        aps[name] = nc.dram_tensor(f"in_{name}_dram", a.shape, _mybir.dt.from_np(a.dtype), kind="ExternalInput").ap()
    n_tables = aps["ids"].shape[1]
    y = nc.dram_tensor("out_0_dram", (aps["ids"].shape[0], 1), _mybir.dt.float32, kind="ExternalOutput").ap()
    dlrm_tower_kernel(nc, aps["r_dense_features"], aps["ids"], [aps[f"tbl_{f}"] for f in range(n_tables)],
                      aps["W_top1"], aps["b_top1"], aps["W_top2"], aps["b_top2"], aps["W_top3"], y)
    r = _run(nc, [arrays], core_ids=[0])
    return r.results[0]["out_0_dram"]
```

```python
import concourse.bass as bass
from concourse import mybir
from contextlib import ExitStack


def dlrm_tower_kernel(nc, dense, ids, tables, W_top1, b_top1, W_top2, b_top2, W_top3, y):
    fp32 = mybir.dt.float32
    fp32r = mybir.dt.float32r
    fp16 = mybir.dt.float16
    int32 = mybir.dt.int32
    ALU = mybir.AluOpType
    ACT = mybir.ActivationFunctionType

    P = 128
    B, D = dense.shape
    F = len(tables)
    ITEMS = F + 1
    N1, N2 = W_top1.shape[1], W_top2.shape[1]
    N = B // P
    T = 2
    S = N // T
    BS = T * P
    BANK = 512
    GS = 4
    SLOT = P // GS
    GT = P // GS
    FG = 8
    GFILLS = GT // FG
    assert GFILLS % 2 == 0
    HALF = T * GFILLS // 2

    MATMUL_TABLES = (12, 13, 14, 15, 17, 18, 20)
    L = len(MATMUL_TABLES)
    EARLY = 5
    L0 = 4
    PAIRED = 2
    LP = -(-L // PAIRED)
    OH = 3
    assert L0 == 2 * PAIRED and LP == OH + 1
    V = tables[MATMUL_TABLES[0]].shape[0]
    VC = -(-V // P)
    VP = V // VC
    assert VC * VP == V and V <= 2048 and all(tables[f].shape[0] == V for f in MATMUL_TABLES)

    QUAD = 4
    gathered = [f for f in range(F) if f not in MATMUL_TABLES]
    turned_items = gathered + [F]
    QUADS = -(-len(turned_items) // QUAD)
    TF = T * QUADS
    quad = [turned_items[QUAD * k:QUAD * k + QUAD] for k in range(QUADS)]
    extra = list(MATMUL_TABLES[L0:])
    quad += [extra[k:k + QUAD] for k in range(0, len(extra), QUAD)]
    QUADS0 = len(quad)
    TF0 = T * QUADS0
    assert TF % 2 == 0 and TF0 % 2 == 0 and QUADS == 5
    START_TURNED = (0, 2, 3, 4)
    place = gathered + extra

    def runs(items):
        out = []
        for j, f in enumerate(items):
            if out and out[-1][1] + out[-1][2] == f:
                out[-1][2] += 1
            else:
                out.append([j, f, 1])
        return out

    PAIRS = F * (F - 1) // 2
    Z = F + PAIRS
    ZC = 3
    ZK = Z // ZC
    assert ZC * ZK == Z and ZK <= P
    pair_at = [F + f * (F - 1) - f * (f - 1) // 2 for f in range(F)]
    M1, M2 = N1 // P, N2 // P

    def is_first(s):
        return isinstance(s, int) and s == 0

    def quads_of(s):
        return QUADS0 if is_first(s) else QUADS

    def tables_of(s):
        return L0 if is_first(s) else L

    def turned_after(s, j):
        n, m = tables_of(s), quads_of(s)
        return [k for k in range(m) if k * (n - 1) // m == j]

    def fills_before(s):
        return 0 if is_first(s) else TF * s + TF0 - TF

    def lookups_before(s):
        return 0 if is_first(s) else L * s + L0 - L

    def pairs_before(s):
        return 0 if is_first(s) else LP * s + L0 // PAIRED - LP

    def in_pair(q):
        return min(PAIRED, L - PAIRED * q)

    ctx = ExitStack()
    with ctx:
        def sb(name, shape, dt=fp32):
            return ctx.enter_context(nc.sbuf_tensor(name, shape, dt))

        def pb(name, shape):
            return ctx.enter_context(nc.psum_tensor(name, shape, fp32))

        def sem(name):
            return ctx.enter_context(nc.semaphore(name))

        ids_sb = sb("ids_sb", [P, T, F], int32)
        ids_mm = sb("ids_mm", [P, T, F], int32)
        ids16 = sb("ids16", [P, T, F], fp16)
        rows = [sb(f"rows{j}", [P, len(place), D]) for j in range(2)]
        dense_sb = sb("dense_sb", [P, T, D])
        eT = sb("eT", [P, T, GT, GS, SLOT])
        dT = sb("dT", [P, BS])
        table_hi = sb("table_hi", [VP, L, VC, D], fp32r)
        table_lo = sb("table_lo", [VP, L, VC, D], fp32r)
        row_of = sb("row_of", [VP, VC])
        onehot = [sb(f"onehot{q}", [VP, VC, in_pair(q), BS], fp32r) for q in range(OH)]
        gram_sb = [sb(f"gram_sb{j}", [P, ITEMS, GT]) for j in range(2)]
        gram_i = sb("gram_i", [P, ITEMS, SLOT])
        feats = [sb(f"feats{j}", [P, Z]) for j in range(2)]
        featsT = sb("featsT", [ZK, ZC, P])
        h1T = sb("h1T", [P, M1, P])
        h2T = sb("h2T", [P, M2, P])
        y_sb = sb("y_sb", [P, N])
        w1 = sb("w1", [ZK, ZC, N1])
        w1s = sb("w1s", [P, N1])
        w2 = sb("w2", [P, M1, N2])
        w3 = sb("w3", [P, M2])
        b1 = sb("b1", [P, M1])
        b2 = sb("b2", [P, M2])
        ident = sb("ident", [P, P])
        ident16 = sb("ident16", [P, P], fp16)
        RAW = 2
        raw_table = sb("raw_table", [VP, RAW, VC, D])
        w1d = sb("w1d", [P, N1])

        tp = [pb(f"tp{j}", [P, QUAD, P]) for j in range(2)]
        gm = [pb(f"gm{j}", [P, FG, BANK // FG]) for j in range(2)]
        mx = [pb(f"mx{j}", [P, BANK]) for j in range(2)]
        idb = [pb(f"idb{j}", [P, PAIRED, BS]) for j in range(2)]

        ids_in = [sem(f"ids_in{t}") for t in range(T)]
        ids_mm_in = sem("ids_mm_in")
        dense_in = [sem(f"dense_in{t}") for t in range(T)]
        table_in = [sem(f"table_in{j}") for j in range(RAW)]
        w1_in = sem("w1_in")
        w1d_in = sem("w1d_in")
        rest_in = sem("rest_in")
        y_out = sem("y_out")
        rows_in = [[sem(f"rows_in{j}_{k}") for k in range(QUADS0)] for j in range(2)]
        pool_steps = sem("pool_steps")
        ident_zero = sem("ident_zero")
        ident_ok = sem("ident_ok")
        row_of_ok = sem("row_of_ok")
        ident16_ok = sem("ident16_ok")
        slots_zero = sem("slots_zero")
        w1s_ok = sem("w1s_ok")
        hi_ok = sem("hi_ok")
        lo_ok = sem("lo_ok")
        ids16_ok = sem("ids16_ok")
        ids_spread = sem("ids_spread")
        onehot_ok = sem("onehot_ok")
        looked_up = sem("looked_up")
        looked_copied = sem("looked_copied")
        turned = sem("turned")
        turned_copied = sem("turned_copied")
        gram_done = sem("gram_done")
        gram_copied = sem("gram_copied")
        gram_copied_act = sem("gram_copied_act")
        gram_turned = sem("gram_turned")
        feats_ok = sem("feats_ok")
        feats_turned = sem("feats_turned")
        featsT_copied = sem("featsT_copied")
        h1_done = sem("h1_done")
        h1_copied = sem("h1_copied")
        h2_done = sem("h2_done")
        h2_copied = sem("h2_copied")
        y_done = sem("y_done")
        y_copied = sem("y_copied")

        block = ctx.enter_context(nc.Block())

        def blocks(eng, body):
            body(0, True, False)
            with eng.Fori(1, S - 1) as s:
                body(s, False, False)
            body(S - 1, False, True)

        @block.sync
        def _(sp):
            ids_t = ids.rearrange("(p n) f -> p n f", n=N)
            dense_t = dense.rearrange("(p n) d -> p n d", n=N)
            table_t = [tables[f].rearrange("(p c) d -> p c d", c=VC) for f in MATMUL_TABLES]
            for t in range(T):
                sp.dma_start(ids_sb[:, t, :], ids_t[:, t, :]).then_inc(ids_in[t], 16)
            sp.dma_start(ids_mm[:, :, :], ids_t[:, 0:T, :]).then_inc(ids_mm_in, 16)
            for j in range(L):
                if j >= RAW:
                    sp.wait_ge(hi_ok, j - RAW + 1)
                    sp.wait_ge(lo_ok, j - RAW + 1)
                sp.dma_start(raw_table[:, j % RAW], table_t[j]).then_inc(table_in[j % RAW], 16)
                if j == 1:
                    for t in range(T):
                        sp.dma_start(dense_sb[:, t, :], dense_t[:, t, :]).then_inc(dense_in[t], 16)

            def next_ids(s):
                sp.wait_ge(ids16_ok, s)
                sp.dma_start(ids_mm[:, :, :], ids_t[:, bass.ds(T * s, T), :]).then_inc(ids_mm_in, 16)

            next_ids(1)
            sp.wait_ge(rows_in[0][QUADS0 - 1], 16 * len(quad[QUADS0 - 1]))
            sp.dma_start(w1s[:, :], W_top1[0:D, :]).then_inc(w1d_in, 16)
            sp.dma_start(w1d[:, :], W_top1[D + Z:D + Z + D, :]).then_inc(w1d_in, 16)
            sp.dma_start(w1[:, :, :], W_top1[D:D + Z, :].rearrange("(k p) n -> p k n", p=ZK)).then_inc(w1_in, 16)
            sp.dma_start(w2[:, :, :], W_top2.rearrange("(k p) n -> p k n", p=P)).then_inc(rest_in, 16)
            with nc.allow_non_contiguous_dma(reason="a few hundred words, once"):
                sp.dma_start(w3[:, :], W_top3.rearrange("(k p) n -> p (k n)", p=P)).then_inc(rest_in, 16)
                sp.dma_start(b1[:, :], b_top1.rearrange("(k p) -> p k", p=P)).then_inc(rest_in, 16)
                sp.dma_start(b2[:, :], b_top2.rearrange("(k p) -> p k", p=P)).then_inc(rest_in, 16)

            def next_tiles(s):
                for t in range(T):
                    sp.wait_ge(turned, fills_before(s - 1) + quads_of(s - 1) * (t + 1))
                    sp.dma_start(ids_sb[:, t:t + 1, :], ids_t[:, bass.ds(T * s + t, 1), :]).then_inc(ids_in[t], 16)
                    sp.dma_start(dense_sb[:, t:t + 1, :],
                                 dense_t[:, bass.ds(T * s + t, 1), :]).then_inc(dense_in[t], 16)

            next_tiles(1)
            with sp.Fori(2, S) as s:
                next_ids(s)
                next_tiles(s)
            sp.wait_ge(y_copied, N)
            sp.dma_start(y.rearrange("(p n) c -> p (n c)", n=N), y_sb[:, :]).then_inc(y_out, 16)
            sp.wait_ge(y_out, 16)

        @block.gpsimd
        def _(pool):
            pool.iota(row_of[:, :], pattern=[[1, VC]], base=0, channel_multiplier=VC,
                      allow_small_or_imprecise_dtypes=True).then_inc(row_of_ok, 1)
            pool.memset(ident[:, :], 0.0).then_inc(ident_zero, 1)
            pool.wait_ge(ident_zero, 1)
            pool.affine_select(out=ident[:, :], in_=ident[:, :], compare_op=ALU.not_equal, fill=1.0,
                               base=0, pattern=[[-1, P]], channel_multiplier=1).then_inc(ident_ok, 1)

            def gathers(s):
                for t in range(T):
                    pool.wait_ge(ids_in[t], 16 * s + 16)
                    pool.sem_inc(pool_steps, 1)
                    for k in range(quads_of(s)):
                        if not is_first(s):
                            pool.wait_ge(turned, fills_before(s - 1) + quads_of(s - 1) * t + k + 1)
                            pool.sem_inc(pool_steps, 1)
                        for f in quad[k]:
                            if f < F:
                                pool.indirect_dma_start(
                                    rows[t % 2][:, place.index(f), :], None, tables[f],
                                    bass.IndirectOffsetOnAxis(ids_sb[:, t, f:f + 1], 0)
                                ).then_inc(rows_in[t % 2][k], 16)

            gathers(0)
            gathers(1)
            with pool.Fori(2, S) as s:
                gathers(s)

        @block.tensor
        def _(pe):
            def shared_bank(n, fill, s_next):
                if fill >= 2:
                    if fill == 2:
                        pe.wait_ge(featsT_copied, n + 1)
                    elif fill <= 2 + M1:
                        pe.wait_ge(h1_copied, M1 * n + fill - 2)
                    else:
                        pe.wait_ge(h2_copied, M2 * n + fill - 2 - M1)
                elif s_next is not None:
                    pe.wait_ge(looked_copied, lookups_before(s_next) + tables_of(s_next) - 1 + fill)
                elif not is_first(n):
                    if fill == 0:
                        pe.wait_ge(h2_copied, M2 * n)
                    else:
                        pe.wait_ge(y_copied, n)
                return mx[fill % 2]

            def spread_ids(s, q):
                pe.wait_ge(ids16_ok, s + 1)
                if q >= 2:
                    pe.wait_ge(onehot_ok, VC * (pairs_before(s) + q - 1))
                elif not is_first(s):
                    pe.wait_ge(onehot_ok, VC * pairs_before(s))
                for j in range(in_pair(q)):
                    f = MATMUL_TABLES[PAIRED * q + j]
                    for t in range(T):
                        last_mm = pe.matmul(idb[q % 2][:, j, P * t:P * t + P],
                                            ids16[:, t, f:f + 1].to_broadcast([P, P]), ident16[:, :],
                                            start=True, stop=True)
                last_mm.then_inc(ids_spread, 1)

            def look_up(s, j):
                looked = mx[(j + tables_of(s)) % 2][:, 0:BS]
                if is_first(s):
                    pe.wait_ge(hi_ok, j + 1)
                    pe.wait_ge(lo_ok, j + 1)
                if j >= 2:
                    pe.wait_ge(looked_copied, lookups_before(s) + j - 1)
                elif not is_first(s):
                    if (j + tables_of(s)) % 2 == 0:
                        pe.wait_ge(h2_copied, M2 * (T * s - 1))
                    else:
                        pe.wait_ge(y_copied, T * s - 1)
                q, h = j // PAIRED, j % PAIRED
                for c in range(VC):
                    pe.wait_ge(onehot_ok, VC * (pairs_before(s) + q) + c + 1)
                    pe.matmul(looked, table_hi[:, j, c, :], onehot[q % OH][:, c, h, :], start=(c == 0), stop=False)
                    last_mm = pe.matmul(looked, table_lo[:, j, c, :], onehot[q % OH][:, c, h, :],
                                        start=False, stop=(c == VC - 1))
                last_mm.then_inc(looked_up, 1)

            def turn(s, first, t, k):
                n = quads_of(s) * t + k
                if not (first and n < 2):
                    pe.wait_ge(turned_copied, fills_before(s) + n - 1)
                pe.wait_ge(rows_in[t % 2][k], 16 * sum(f < F for f in quad[k]) * (s + 1))
                if k == QUADS - 1:
                    pe.wait_ge(dense_in[t], 16 * s + 16)
                for j, f in enumerate(quad[k]):
                    src = rows[t % 2][:, place.index(f), :] if f < F else dense_sb[:, t, :]
                    last_mm = pe.transpose(tp[n % 2][:, j, :], src, ident[:, :])
                last_mm.then_inc(turned, 1)

            def gram(s, first, t, between=None):
                pe.wait_ge(turned_copied, fills_before(s) + quads_of(s) * (t + 1))
                if t == 0:
                    pe.wait_ge(looked_copied, lookups_before(s) + tables_of(s))
                for j in range(GFILLS):
                    n = GFILLS * t + j
                    if not (first and n < 2):
                        pe.wait_ge(gram_copied_act if n % 2 == 0 else gram_copied, HALF * s + n // 2)
                    for g in range(FG):
                        for c in range(GS):
                            items = eT[:, t, FG * j + g, c, :]
                            last_mm = pe.matmul(gm[n % 2][SLOT * c:SLOT * c + SLOT, g, 0:ITEMS], items,
                                                items[:, 0:ITEMS], start=True, stop=True)
                    last_mm.then_inc(gram_done, 1)
                    if between:
                        between(j)

            def turn_feats(n, t, s_next=None):
                bank = shared_bank(n, 0, s_next)
                pe.wait_ge(feats_ok, n + 1)
                for k in range(ZC):
                    last_mm = pe.transpose(bank[0:ZK, P * k:P * k + P], feats[t][:, ZK * k:ZK * k + ZK],
                                           ident[:, :])
                last_mm.then_inc(feats_turned, 1)

            def layer1(n, t, chunks=range(M1), s_next=None):
                for m in chunks:
                    acc = shared_bank(n, 1 + m, s_next)[:, 0:P]
                    pe.matmul(acc, w1s[:, P * m:P * m + P], dT[:, P * t:P * t + P], start=True, stop=False)
                    if m == 0:
                        pe.wait_ge(featsT_copied, n + 1)
                    for k in range(ZC):
                        last_mm = pe.matmul(acc, w1[:, k, P * m:P * m + P], featsT[:, k, :],
                                            start=False, stop=(k == ZC - 1))
                    last_mm.then_inc(h1_done, 1)

            def layer2(n, chunks=range(M2)):
                for m in chunks:
                    acc = shared_bank(n, 1 + M1 + m, None)[:, 0:P]
                    for k in range(M1):
                        if m == 0:
                            pe.wait_ge(h1_copied, M1 * n + k + 1)
                        last_mm = pe.matmul(acc, w2[:, k, P * m:P * m + P], h1T[:, k, :],
                                            start=(k == 0), stop=(k == M1 - 1))
                    last_mm.then_inc(h2_done, 1)

            def layer3(n):
                bank = shared_bank(n, 1 + M1 + M2, None)
                for k in range(M2):
                    pe.wait_ge(h2_copied, M2 * n + k + 1)
                    last_mm = pe.matmul(bank[:, 0:1], h2T[:, k, :], w3[:, k:k + 1],
                                        start=(k == 0), stop=(k == M2 - 1))
                last_mm.then_inc(y_done, 1)

            def whole_block(s, first, last):
                quads = quads_of(s)

                def between(j):
                    if not last and j < 2:
                        spread_ids(s + 1, j)
                    if j == GFILLS // 2:
                        turn(s, first, 1, 0)

                gram(s, first, 0, between)
                if not first:
                    layer1(T * s - 1, 1, range(M1 // 2, M1))
                    turn(s, first, 1, 1)
                    layer2(T * s - 1)
                    turn(s, first, 1, 2)
                    layer3(T * s - 1)
                else:
                    turn(s, first, 1, 1)
                    turn(s, first, 1, 2)
                turn_feats(T * s, 0)
                turn(s, first, 1, 3)
                if first:
                    pe.wait_ge(w1s_ok, 1)
                    pe.wait_ge(w1_in, 16)
                    pe.wait_ge(rest_in, 64)
                layer1(T * s, 0, range(M1 // 2))
                turn(s, first, 1, 4)
                if not last:
                    layer1(T * s, 0, range(M1 // 2, M1))
                    for k in range(5, quads):
                        turn(s, first, 1, k)
                    spread_ids(s + 1, 2)

                    def between(j):
                        if j < M2:
                            layer2(T * s, [j])
                        if j == M2:
                            layer3(T * s)
                        if j == 1:
                            spread_ids(s + 1, 3)

                    gram(s, first, 1, between)
                    if first:
                        pe.wait_ge(hi_ok, L)
                        pe.wait_ge(lo_ok, L)
                    for j in range(tables_of(s + 1)):
                        look_up(s + 1, j)
                        for k in turned_after(s + 1, j):
                            turn(s + 1, False, 0, k)
                    turn_feats(T * s + 1, 1, s + 1)
                    layer1(T * s + 1, 1, range(M1 // 2), s + 1)
                else:
                    for k in range(5, quads):
                        turn(s, first, 1, k)

                    def between(j):
                        if j == 1:
                            layer1(T * s, 0, [M1 // 2])

                    gram(s, first, 1, between)
                    layer1(T * s, 0, range(M1 // 2 + 1, M1))
                    layer2(T * s)
                    layer3(T * s)
                    turn_feats(T * s + 1, 1)
                    layer1(T * s + 1, 1)

            pe.wait_ge(ident16_ok, 1)
            spread_ids(0, 0)
            spread_ids(0, 1)
            pe.wait_ge(ident_ok, 1)
            for j in range(L0):
                look_up(0, j)
                if j > 0:
                    for k in range(START_TURNED[j - 1], START_TURNED[j]):
                        turn(0, True, 0, k)
            for k in range(START_TURNED[L0 - 1], QUADS0):
                turn(0, True, 0, k)
            pe.wait_ge(slots_zero, 1)
            blocks(pe, whole_block)
            layer2(N - 1)
            layer3(N - 1)

        @block.scalar
        def _(act):
            def table_high(j):
                act.wait_ge(table_in[j % RAW], 16 * (j // RAW + 1))
                act.activation(table_hi[:, j, :, :], raw_table[:, j % RAW], ACT.Copy).then_inc(hi_ok, 1)

            def looked_out(s, j):
                act.wait_ge(looked_up, lookups_before(s) + j + 1)
                f = MATMUL_TABLES[j]
                act.activation(eT[:, :, :, :, f].rearrange("p t i c -> p t c i"),
                               mx[(j + tables_of(s)) % 2][:, 0:BS].rearrange("p (t c i) -> p t c i", t=T, c=GS),
                               ACT.Copy).then_inc(looked_copied, 1)

            def items_out(s, first, t, k):
                n = quads_of(s) * t + k
                act.wait_ge(turned, fills_before(s) + n + 1)
                if k == QUADS - 1:
                    act.activation(dT[:, P * t:P * t + P], tp[n % 2][:, len(quad[k]) - 1, :], ACT.Copy)
                for j, f, m in runs(quad[k]):
                    last_copy = act.activation(
                        eT[:, t, :, :, f:f + m].rearrange("p i c f -> p f c i"),
                        tp[n % 2][:, j:j + m, :].rearrange("p f (c i) -> p f c i", c=GS), ACT.Copy)
                last_copy.then_inc(turned_copied, 1)

            def grams_out(s, first, t, between=None):
                for j in range(GFILLS):
                    n = GFILLS * t + j
                    if j % 2 == 0:
                        act.wait_ge(gram_done, T * GFILLS * s + n + 1)
                        if j == 0 and not (first and t < 2):
                            act.wait_ge(gram_turned, T * s + t - 1)
                        act.activation(gram_sb[t % 2][:, :, FG * j:FG * j + FG].rearrange("p f i -> p i f"),
                                       gm[n % 2][:, :, 0:ITEMS], ACT.Copy).then_inc(gram_copied_act, 1)
                    if between:
                        between(j)

            def feats_out(n):
                act.wait_ge(feats_turned, n + 1)
                act.activation(featsT[:, :, :], mx[0][0:ZK, 0:ZC * P].rearrange("p (k b) -> p k b", k=ZC),
                               ACT.Copy).then_inc(featsT_copied, 1)

            def h1_out(n, chunks=range(M1)):
                for m in chunks:
                    act.wait_ge(h1_done, M1 * n + m + 1)
                    act.activation(h1T[:, m, :], mx[(1 + m) % 2][:, 0:P], ACT.Relu,
                                   bias=b1[:, m:m + 1]).then_inc(h1_copied, 1)

            def h2_out(n, chunks=range(M2)):
                for m in chunks:
                    act.wait_ge(h2_done, M2 * n + m + 1)
                    act.activation(h2T[:, m, :], mx[(1 + M1 + m) % 2][:, 0:P], ACT.Relu,
                                   bias=b2[:, m:m + 1]).then_inc(h2_copied, 1)

            def y_out_of_psum(n):
                act.wait_ge(y_done, n + 1)
                act.activation(y_sb[:, n:n + 1] if isinstance(n, int) else y_sb[:, bass.ds(n, 1)],
                               mx[(1 + M1 + M2) % 2][:, 0:1], ACT.Copy).then_inc(y_copied, 1)

            def whole_block(s, first, last):
                quads = quads_of(s)

                def between(j):
                    if j == GFILLS // 2:
                        items_out(s, first, 1, 0)

                grams_out(s, first, 0, between)
                if first:
                    for j in range(EARLY, L):
                        table_high(j)
                if not first:
                    h1_out(T * s - 1, range(M1 // 2, M1))
                    items_out(s, first, 1, 1)
                    h2_out(T * s - 1)
                    items_out(s, first, 1, 2)
                    y_out_of_psum(T * s - 1)
                else:
                    items_out(s, first, 1, 1)
                    items_out(s, first, 1, 2)
                feats_out(T * s)
                items_out(s, first, 1, 3)
                if first:
                    act.wait_ge(rest_in, 64)
                h1_out(T * s, range(M1 // 2))
                items_out(s, first, 1, 4)
                if not last:
                    h1_out(T * s, range(M1 // 2, M1))
                    for k in range(5, quads):
                        items_out(s, first, 1, k)

                    def between(j):
                        if j < M2:
                            h2_out(T * s, [j])
                        if j == M2:
                            y_out_of_psum(T * s)

                    grams_out(s, first, 1, between)
                    for j in range(tables_of(s + 1)):
                        looked_out(s + 1, j)
                        for k in turned_after(s + 1, j):
                            items_out(s + 1, False, 0, k)
                    feats_out(T * s + 1)
                    h1_out(T * s + 1, range(M1 // 2))
                else:
                    for k in range(5, quads):
                        items_out(s, first, 1, k)

                    def between(j):
                        if j == 1:
                            h1_out(T * s, [M1 // 2])

                    grams_out(s, first, 1, between)
                    h1_out(T * s, range(M1 // 2 + 1, M1))
                    h2_out(T * s)
                    y_out_of_psum(T * s)
                    feats_out(T * s + 1)
                    h1_out(T * s + 1)

            for j in range(EARLY):
                table_high(j)
                if 1 <= j <= L0:
                    looked_out(0, j - 1)
                    if j > 1:
                        for k in range(START_TURNED[j - 2], START_TURNED[j - 1]):
                            items_out(0, True, 0, k)
            for k in range(START_TURNED[L0 - 1], QUADS0):
                items_out(0, True, 0, k)
            blocks(act, whole_block)
            h2_out(N - 1)
            y_out_of_psum(N - 1)

        @block.vector
        def _(dve):
            def table_low(j):
                dve.wait_ge(hi_ok, j + 1)
                dve.tensor_tensor(table_lo[:, j, :, :], raw_table[:, j % RAW], table_hi[:, j, :, :].bitcast(fp32),
                                  ALU.subtract).then_inc(lo_ok, 1)

            def convert_ids(s):
                dve.wait_ge(ids_mm_in, 16 * s + 16)
                if not is_first(s):
                    dve.wait_ge(ids_spread, pairs_before(s))
                for j, f, m in runs(MATMUL_TABLES):
                    last_op = dve.tensor_copy(ids16[:, :, f:f + m], ids_mm[:, :, f:f + m])
                last_op.then_inc(ids16_ok, 1)

            def compare_ids(s, q, chunks=range(VC)):
                dve.wait_ge(ids_spread, pairs_before(s) + q + 1)
                for c in chunks:
                    dve.tensor_scalar(onehot[q % OH][:, c, 0:in_pair(q), :], idb[q % 2][0:VP, 0:in_pair(q), :],
                                      row_of[:, c:c + 1], None, ALU.is_equal).then_inc(onehot_ok, 1)

            def grams_out(s, first, t, pair):
                for j in range(GFILLS):
                    n = GFILLS * t + j
                    if j % 2 == 1:
                        dve.wait_ge(gram_done, T * GFILLS * s + n + 1)
                        dve.tensor_copy(gram_sb[t % 2][:, :, FG * j:FG * j + FG].rearrange("p f i -> p i f"),
                                        gm[n % 2][:, :, 0:ITEMS]).then_inc(gram_copied, 1)
                    if pair is not None:
                        compare_ids(s + 1, pair, range(j, j + 1))

            def gram_turn(s, first, t):
                dve.wait_ge(gram_copied, HALF * s + GFILLS // 2 * (t + 1))
                dve.wait_ge(gram_copied_act, HALF * s + GFILLS // 2 * (t + 1))
                if not (first and t == 0):
                    dve.wait_ge(feats_ok, T * s + t)
                dve.transpose(gram_i[:, :, :].rearrange("p g f -> p (g f)"),
                              gram_sb[t % 2][:, :, :].rearrange("p g i -> p (g i)")).then_inc(gram_turned, 1)

            def feats_out(s, first, t):
                dve.wait_ge(gram_turned, T * s + t + 1)
                if not (first and t < 2):
                    dve.wait_ge(feats_turned, T * s + t - 1)
                z = feats[t % 2]
                for f in range(F - 1):
                    dve.tensor_copy(z[:, pair_at[f]:pair_at[f] + F - 1 - f], gram_i[:, f, f + 1:F])
                dve.tensor_copy(z[:, 0:F], gram_i[:, F, 0:F]).then_inc(feats_ok, 1)

            def whole_block(s, first, last):
                if not last:
                    convert_ids(s + 1)
                    dve.wait_ge(looked_up, lookups_before(s + 1))
                grams_out(s, first, 0, None if last else 0)
                gram_turn(s, first, 0)
                feats_out(s, first, 0)
                if first:
                    dve.wait_ge(w1d_in, 32)
                    dve.tensor_tensor(w1s[:, :], w1s[:, :], w1d[:, :], ALU.add).then_inc(w1s_ok, 1)
                    for j in range(EARLY, L):
                        table_low(j)
                if not last:
                    compare_ids(s + 1, 0, range(GFILLS, VC))
                    compare_ids(s + 1, 1)
                grams_out(s, first, 1, None if last else 2)
                gram_turn(s, first, 1)
                feats_out(s, first, 1)
                if not last:
                    compare_ids(s + 1, 2, range(GFILLS, VC))
                    dve.wait_ge(looked_up, lookups_before(s + 1) + PAIRED)
                    compare_ids(s + 1, 3)

            dve.memset(eT[:, :, :, :, ITEMS:SLOT].rearrange("p t i c f -> p (t i c) f"), 0.0).then_inc(slots_zero, 1)
            dve.wait_ge(ident_ok, 1)
            dve.tensor_copy(ident16[:, :], ident[:, :]).then_inc(ident16_ok, 1)
            convert_ids(0)
            dve.wait_ge(row_of_ok, 1)
            for j in range(EARLY):
                table_low(j)
                if j < L0 // PAIRED:
                    compare_ids(0, j)
            blocks(dve, whole_block)


def kernel(**inputs):
    import numpy as _np
    import concourse.bacc as _bacc
    from concourse import mybir as _mybir
    from concourse.bass_utils import run_bass_kernel_spmd as _run

    nc = _bacc.Bacc("TRN2", target_bir_lowering=False, num_devices=1)
    arrays, aps = {}, {}
    for name in inputs:
        a = _np.ascontiguousarray(inputs[name])
        arrays[f"in_{name}_dram"] = a
        aps[name] = nc.dram_tensor(f"in_{name}_dram", a.shape, _mybir.dt.from_np(a.dtype), kind="ExternalInput").ap()
    n_tables = aps["ids"].shape[1]
    y = nc.dram_tensor("out_0_dram", (aps["ids"].shape[0], 1), _mybir.dt.float32, kind="ExternalOutput").ap()
    dlrm_tower_kernel(nc, aps["r_dense_features"], aps["ids"], [aps[f"tbl_{f}"] for f in range(n_tables)],
                      aps["W_top1"], aps["b_top1"], aps["W_top2"], aps["b_top2"], aps["W_top3"], y)
    r = _run(nc, [arrays], core_ids=[0])
    return r.results[0]["out_0_dram"]
```
